# Optimizing a Trainium2 kernel written in Bass

```python
import numpy as np
import jax
import jax.numpy as jnp

def _softmax(x, axis=-1):
    return jax.nn.softmax(x, axis=axis)

def _gelu(x):
    return jax.nn.gelu(x, approximate=True)

def _silu(x):
    return jax.nn.silu(x)

def _sigmoid(x):
    return jax.nn.sigmoid(x)

def _layernorm(x, axis=-1, eps=1e-05):
    m = jnp.mean(x, axis=axis, keepdims=True)
    v = jnp.var(x, axis=axis, keepdims=True)
    return (x - m) / jnp.sqrt(v + eps)

def _scatter_add(tgt, idx, src, axis=0):
    return tgt.at[idx].add(src)

def _segment_sum(src, seg, n):
    return jax.ops.segment_sum(src, seg, n)
kernel_name = 'mk_rec_standalone_d1_rec_r8_6164b9'

def setup_inputs(seed: int=0):
    np.random.seed(seed)
    _w = jnp.asarray

    def _rec_inputs():
        import jax
        import jax.numpy as jnp
        _rk = jax.random.key(seed)
        r_x = -7.10856e-05 + 0.999911 * jax.random.normal(jax.random.fold_in(_rk, 1), (2048, 64, 128), jnp.float32)
        return r_x
    r_x = _rec_inputs()

    def _L0_rec_setup():
        import jax, jax.numpy as jnp
        import numpy as np
        B, M, D, DP = (1024, 64, 128, 128)
        key = jax.random.key(seed)
        kx, kq, kk, kv, kr = jax.random.split(key, 5)
        scale = 1.0 / np.sqrt(D)
        return {'x': jax.random.normal(kx, (B, M, D), dtype=jnp.float32), 'Wq': jax.random.normal(kq, (D, DP), dtype=jnp.float32) * scale, 'Wk': jax.random.normal(kk, (D, DP), dtype=jnp.float32) * scale, 'Wv': jax.random.normal(kv, (D, DP), dtype=jnp.float32) * scale, 'Wr': jax.random.normal(kr, (D, DP), dtype=jnp.float32) * scale}
    _L0_rec_all = _L0_rec_setup()
    _L0_rec_in = {k: v for k, v in _L0_rec_all.items() if k in ('Wq', 'Wk', 'Wv', 'Wr')}
    del _L0_rec_all
    return {'r_x': r_x, 'L0_rec_Wq': _L0_rec_in['Wq'], 'L0_rec_Wk': _L0_rec_in['Wk'], 'L0_rec_Wv': _L0_rec_in['Wv'], 'L0_rec_Wr': _L0_rec_in['Wr']}

def reference(r_x, L0_rec_Wq, L0_rec_Wk, L0_rec_Wv, L0_rec_Wr):
    import jax
    import jax.numpy as jnp

    def _L0_rec_ref(x, Wq, Wk, Wv, Wr):
        import jax, jax.numpy as jnp
        import numpy as np
        B, M, D, DP = (1024, 64, 128, 128)
        q = jnp.einsum('bmd,de->bme', x, Wq)
        k = jnp.einsum('bmd,de->bme', x, Wk)
        v = jnp.einsum('bmd,de->bme', x, Wv)
        r = jnp.einsum('bmd,de->bme', x, Wr)
        scores = jnp.einsum('bme,bne->bmn', q, k)
        alphas = jax.nn.softmax(scores, axis=2)
        new_e = jnp.einsum('bmn,bne->bme', alphas, v)
        return jax.nn.relu(r + new_e)
    y = _L0_rec_ref(r_x, L0_rec_Wq, L0_rec_Wk, L0_rec_Wv, L0_rec_Wr)
    return y

_drawn_inputs = setup_inputs


def setup_inputs(seed=0):
    import zlib

    import numpy as np

    out = dict(_drawn_inputs(seed))
    spreads = {}
    factors = {}
    for name, (base, spread) in spreads.items():
        noise = np.random.default_rng([zlib.crc32(name.encode()), seed]).standard_normal(out[name].shape)
        drawn = base * np.exp(spread * noise) if base else spread * noise
        out[name] = jnp.asarray(drawn.astype(out[name].dtype))
    for name, factor in factors.items():
        out[name] = (out[name] * factor).astype(out[name].dtype)
    return out
```

```python
from contextlib import ExitStack

import concourse.bass as bass
from concourse import mybir


def recommender_self_attention(
    nc: bass.Bass,
    x: bass.AP,
    Wq: bass.AP,
    Wk: bass.AP,
    Wv: bass.AP,
    Wr: bass.AP,
    out: bass.AP,
):
    fp32 = mybir.dt.float32
    fp32r = mybir.dt.float32r
    ALU = mybir.AluOpType
    ACT = mybir.ActivationFunctionType
    AX = mybir.AxisListType

    B, M, D = x.shape
    P = 128
    T = 2
    PAIRS = B * M // (P * T)
    C = 2
    SLOTS = 3
    U = C * SLOTS
    SC, RC, VC, PC = 0, P, 2 * P, 3 * P
    W3 = 3 * P
    ROUND_A = 2
    ROUND_Z = (PAIRS - 2) // U

    x_chunks = x.flatten_outer_dims().rearrange("(c t p) d -> c p t d", p=P, t=C * T)
    out_chunks = out.flatten_outer_dims().rearrange("(c t p) d -> c p t d", p=P, t=C * T)

    with ExitStack() as ctx:
        def sb(name, shape, dtype=fp32):
            return ctx.enter_context(nc.sbuf_tensor(name, shape, dtype))

        def sem(name):
            return ctx.enter_context(nc.semaphore(name))

        w_in = sb("w_in", [P, 4, D])
        w_t = sb("w_t", [P, 2, D])
        ident = sb("ident", [P, P])
        g_hi = sb("g_hi", [P, D], fp32r)
        g_lo = sb("g_lo", [P, D], fp32r)
        x_in = sb("x_in", [P, SLOTS, C * T, D])
        xt_hi = sb("xt_hi", [P, 3, T * P], fp32r)
        xt_lo = sb("xt_lo", [P, 3, T * P], fp32r)
        mv_hi = sb("mv_hi", [P, 2, T, W3], fp32r)
        mv_lo = sb("mv_lo", [P, 2, T, W3], fp32r)
        scores = sb("scores", [P, 2, T, M])
        shifted = sb("shifted", [P, 2, T, M])
        probs = sb("probs", [P, 2, T, M])
        row_max = sb("row_max", [P, 2, T, 1])
        row_sum = sb("row_sum", [P, 2, T, 1])
        row_inv = sb("row_inv", [P, 2, T, 1])
        diag = sb("diag", [P, 2, T, P])
        diag_t = sb("diag_t", [P, 2, T, P])
        v_sb = sb("v_sb", [P, 3, T, D])
        y_out = sb("y_out", [P, SLOTS, C * T, D])

        xt_ps = ctx.enter_context(nc.psum_tensor("xt_ps", [P, 512], fp32))
        t_ps = ctx.enter_context(nc.psum_tensor("t_ps", [P, 512], fp32))
        prod = ctx.enter_context(nc.psum_tensor("prod", [P, 3, T, 512], fp32))

        weights_loaded = sem("weights_loaded")
        ident_ready = sem("ident_ready")
        diag_zero = sem("diag_zero")
        w_t_ready = sem("w_t_ready")
        w_t_copied = sem("w_t_copied")
        g_ready = sem("g_ready")
        g_hi_ready = sem("g_hi_ready")
        w_hi_ready = sem("w_hi_ready")
        split_ready = sem("split_ready")
        x_loaded = [sem(f"x_loaded_{s}") for s in range(SLOTS)]
        y_stored = [sem(f"y_stored_{s}") for s in range(SLOTS)]
        xt_ready = sem("xt_ready")
        xt_hi_ready = sem("xt_hi_ready")
        xt_lo_ready = sem("xt_lo_ready")
        t_ready = sem("t_ready")
        t_hi_ready = sem("t_hi_ready")
        t_lo_ready = sem("t_lo_ready")
        prod_ready = sem("prod_ready")
        scores_copied = sem("scores_copied")
        v_copied = sem("v_copied")
        max_ready = sem("max_ready")
        shift_ready = sem("shift_ready")
        exp_ready = sem("exp_ready")
        sum_ready = sem("sum_ready")
        inv_ready = sem("inv_ready")
        diag_ready = sem("diag_ready")
        pt_ready = sem("pt_ready")
        pt_copied = sem("pt_copied")
        y_ready = sem("y_ready")
        y_copied = sem("y_copied")

        block = ctx.enter_context(nc.Block())

        def exists(j):
            return not isinstance(j, int) or 0 <= j < PAIRS

        def past(j, n):
            return not isinstance(j, int) or j >= n

        def run(engine, step, first, end):
            for i in range(first, ROUND_A * U):
                step(i, i // U, i % U)
            with engine.Fori(ROUND_A, ROUND_Z) as k:
                i = engine.snap(k * U)
                for r in range(U):
                    step(i + r, k, r)
            for i in range(ROUND_Z * U, end):
                step(i, i // U, i % U)

        @block.sync
        def _(sp):
            for n, w in enumerate((Wq, Wk, Wr, Wv)):
                sp.dma_start(w_in[:, n, :], w).then_inc(weights_loaded, 16)

            def load(c, s):
                sp.dma_start(x_in[:, s], x_chunks[c]).then_inc(x_loaded[s], 16)

            def store(c, s):
                sp.wait_ge(y_copied, (c + 1) * C)
                sp.dma_start(out_chunks[c], y_out[:, s]).then_inc(y_stored[s], 16)

            def reload(c, s):
                sp.wait_ge(xt_ready, (c + 1 - SLOTS) * C)
                load(c, s)

            chunks = PAIRS // C
            for c in range(SLOTS):
                load(c, c)
            for c in range(SLOTS, 2 * SLOTS):
                reload(c, c - SLOTS)
            loop_end = chunks // SLOTS * SLOTS
            with sp.Fori(2, chunks // SLOTS) as k:
                for s in range(SLOTS):
                    store((k - 2) * SLOTS + s, s)
                    reload(k * SLOTS + s, s)
            for c in range(loop_end, chunks):
                reload(c, c % SLOTS)
            for c in range(loop_end - 2 * SLOTS, chunks):
                store(c, c % SLOTS)
            for s in range(SLOTS):
                sp.wait_ge(y_stored[s], 16 * len(range(s, chunks, SLOTS)))

        @block.tensor
        def _(pe):
            pe.wait_ge(weights_loaded, 64)
            pe.wait_ge(ident_ready, 1)
            for n in range(2):
                last = pe.transpose(xt_ps[:, n * P:(n + 1) * P], w_in[:, n, :], ident[:])
            last.then_inc(w_t_ready, 1)
            pe.wait_ge(w_t_copied, 1)
            pe.matmul(t_ps[:, 0:D], w_t[:, 1, :], w_t[:, 0, :], start=True, stop=True).then_inc(g_ready, 1)
            pe.wait_ge(split_ready, 2)

            def transpose_x(j, k, r):
                if r % C == 0:
                    pe.wait_ge(x_loaded[r // C], k * 16 + 16)
                if past(j, 1):
                    pe.wait_ge(xt_lo_ready, j)
                for t in range(T):
                    last = pe.transpose(xt_ps[:, t * P:(t + 1) * P], x_in[:, r // C, r % C * T + t, :], ident[:])
                last.then_inc(xt_ready, 1)

            def project_t(j, r):
                pe.wait_ge(xt_hi_ready, j + 1)
                pe.wait_ge(xt_lo_ready, j + 1)
                if past(j, 1):
                    pe.wait_ge(t_lo_ready, j)
                o = t_ps[:, 0:T * P]
                pe.matmul(o, g_hi[:], xt_hi[:, r % 3], start=True, stop=False)
                pe.matmul(o, g_lo[:], xt_hi[:, r % 3], start=False, stop=False)
                pe.matmul(o, g_hi[:], xt_lo[:, r % 3], start=False, stop=True).then_inc(t_ready, 1)

            def transpose_p(j, r):
                pe.wait_ge(diag_ready, j * 2 + 2)
                pe.wait_ge(v_copied, j + 1)
                for t in range(T):
                    last = pe.matmul(prod[:, r % 3, t, PC:PC + P], diag[:, r % 2, t], ident[:],
                                     is_transpose=True, start=False, stop=True, skip_group_check=True)
                last.then_inc(pt_ready, 1)

            def product(j, r):
                pe.wait_ge(t_hi_ready, j + 1)
                pe.wait_ge(t_lo_ready, j + 1)
                if past(j, 3):
                    pe.wait_ge(y_copied, j - 2)
                for t in range(T):
                    o = prod[:, r % 3, t, 0:W3]
                    xh = xt_hi[:, r % 3, t * P:(t + 1) * P]
                    xl = xt_lo[:, r % 3, t * P:(t + 1) * P]
                    pe.matmul(o, xh, mv_hi[:, r % 2, t], start=True, stop=False, skip_group_check=True)
                    pe.matmul(o, xh, mv_lo[:, r % 2, t], start=False, stop=False, skip_group_check=True)
                    last = pe.matmul(o, xl, mv_hi[:, r % 2, t], start=False, stop=False, skip_group_check=True)
                last.then_inc(prod_ready, 1)

            def attend(j, r):
                pe.wait_ge(pt_copied, j + 1)
                for t in range(T):
                    last = pe.matmul(prod[:, r % 3, t, RC:RC + D], diag_t[:, r % 2, t], v_sb[:, r % 3, t],
                                     start=False, stop=True, skip_group_check=True)
                last.then_inc(y_ready, 1)

            def step(i, k, r):
                if exists(i + 2):
                    transpose_x(i + 2, k + (r + 2) // U, (r + 2) % U)
                if exists(i + 1):
                    project_t(i + 1, (r + 1) % U)
                if exists(i - 2):
                    transpose_p(i - 2, (r - 2) % U)
                if exists(i):
                    product(i, r)
                if exists(i - 2):
                    attend(i - 2, (r - 2) % U)

            run(pe, step, -2, PAIRS + 2)

        @block.scalar
        def _(act):
            act.wait_ge(weights_loaded, 64)
            for s in range(2):
                for t in range(T):
                    last = act.copy(mv_hi[:, s, t, RC:W3], w_in[:, 2:4, :].rearrange("p a b -> p (a b)"))
            last.then_inc(w_hi_ready, 1)
            act.wait_ge(w_t_ready, 1)
            act.copy(w_t[:].rearrange("p a b -> p (a b)"), xt_ps[:, 0:2 * P]).then_inc(w_t_copied, 1)
            act.wait_ge(g_ready, 1)
            act.copy(g_hi[:], t_ps[:, 0:D]).then_inc(g_hi_ready, 1)

            def copy_scores(j, r):
                act.wait_ge(prod_ready, j + 1)
                if past(j, 2):
                    act.wait_ge(shift_ready, j - 1)
                for h in range(2):
                    rows = slice(h * M, (h + 1) * M)
                    act.copy(scores[rows, r % 2], prod[rows, r % 3, :, SC + h * M:SC + (h + 1) * M])\
                       .then_inc(scores_copied, 1)

            def copy_v(j, r):
                if past(j, 3):
                    act.wait_ge(y_ready, j - 2)
                act.copy(v_sb[:, r % 3], prod[:, r % 3, :, VC:VC + D]).then_inc(v_copied, 1)

            def round_xt(j, r):
                act.wait_ge(xt_ready, j + 1)
                if past(j, 3):
                    act.wait_ge(prod_ready, j - 2)
                act.copy(xt_hi[:, r % 3], xt_ps[:, 0:T * P]).then_inc(xt_hi_ready, 1)

            def round_t(j, r):
                act.wait_ge(t_ready, j + 1)
                if past(j, 2):
                    act.wait_ge(prod_ready, j - 1)
                act.copy(mv_hi[:, r % 2, :, SC:SC + P],
                         t_ps[:, 0:T * P].rearrange("p (t c) -> p t c", t=T)).then_inc(t_hi_ready, 1)

            def exponentials(j, r):
                act.wait_ge(shift_ready, j + 1)
                if past(j, 2):
                    act.wait_ge(diag_ready, (j - 1) * 2)
                act.activation(probs[:, r % 2], shifted[:, r % 2], ACT.Exp).then_inc(exp_ready, 1)

            def copy_pt(j, r):
                act.wait_ge(pt_ready, j + 1)
                if past(j, 2):
                    act.wait_ge(y_ready, j - 1)
                act.copy(diag_t[:, r % 2], prod[:, r % 3, :, PC:PC + P]).then_inc(pt_copied, 1)

            def step(i, k, r):
                if exists(i - 1):
                    copy_scores(i - 1, (r - 1) % U)
                    copy_v(i - 1, (r - 1) % U)
                if exists(i + 2):
                    round_xt(i + 2, (r + 2) % U)
                if exists(i + 1):
                    round_t(i + 1, (r + 1) % U)
                if exists(i - 1):
                    exponentials(i - 1, (r - 1) % U)
                if exists(i - 2):
                    copy_pt(i - 2, (r - 2) % U)

            run(act, step, -2, PAIRS + 2)

        @block.vector
        def _(dve):
            dve.wait_ge(w_hi_ready, 1)
            for s in range(2):
                for t in range(T):
                    last = dve.tensor_tensor(mv_lo[:, s, t, RC:W3], w_in[:, 2:4, :].rearrange("p a b -> p (a b)"),
                                             mv_hi[:, s, t, RC:W3], ALU.subtract)
            last.then_inc(split_ready, 1)
            dve.wait_ge(g_hi_ready, 1)
            dve.tensor_tensor(g_lo[:], t_ps[:, 0:D], g_hi[:], ALU.subtract).then_inc(split_ready, 1)

            def maximum(j, r):
                dve.wait_ge(scores_copied, j * 2 + 2)
                dve.tensor_reduce(row_max[:, r % 2], scores[:, r % 2], AX.X, ALU.max).then_inc(max_ready, 1)

            def shift(j, r):
                dve.wait_ge(max_ready, j + 1)
                dve.tensor_tensor(shifted[:, r % 2], scores[:, r % 2],
                                  row_max[:, r % 2].broadcast_to([P, T, M]), ALU.subtract).then_inc(shift_ready, 1)

            def rest_of_xt(j, r):
                dve.wait_ge(xt_hi_ready, j + 1)
                dve.tensor_tensor(xt_lo[:, r % 3], xt_ps[:, 0:T * P], xt_hi[:, r % 3],
                                  ALU.subtract).then_inc(xt_lo_ready, 1)

            def rest_of_t(j, r):
                dve.wait_ge(t_hi_ready, j + 1)
                dve.tensor_tensor(mv_lo[:, r % 2, :, SC:SC + P], t_ps[:, 0:T * P].rearrange("p (t c) -> p t c", t=T),
                                  mv_hi[:, r % 2, :, SC:SC + P], ALU.subtract).then_inc(t_lo_ready, 1)

            def sums(j, r):
                dve.wait_ge(exp_ready, j + 1)
                dve.tensor_reduce(row_sum[:, r % 2], probs[:, r % 2], AX.X, ALU.add).then_inc(sum_ready, 1)
                dve.wait_ge(sum_ready, j + 1)
                dve.reciprocal(row_inv[:, r % 2], row_sum[:, r % 2]).then_inc(inv_ready, 1)

            def finish(j, k, r):
                dve.wait_ge(y_ready, j + 1)
                if r % C == 0 and past(j, U):
                    dve.wait_ge(y_stored[r // C], k * 16)
                dve.tensor_scalar(y_out[:, r // C, r % C * T:(r % C + 1) * T], prod[:, r % 3, :, RC:RC + D],
                                  0.0, None, ALU.max).then_inc(y_copied, 1)

            def step(i, k, r):
                if exists(i - 1):
                    maximum(i - 1, (r - 1) % U)
                if exists(i - 3):
                    finish(i - 3, k + (r - 3) // U, (r - 3) % U)
                if exists(i - 1):
                    shift(i - 1, (r - 1) % U)
                if exists(i + 2):
                    rest_of_xt(i + 2, (r + 2) % U)
                if exists(i - 1):
                    sums(i - 1, (r - 1) % U)
                if exists(i + 1):
                    rest_of_t(i + 1, (r + 1) % U)

            run(dve, step, -2, PAIRS + 3)

        @block.gpsimd
        def _(pool):
            pool.memset(ident[:], 0.0).then_inc(diag_zero, 1)
            pool.memset(diag[:], 0.0).then_inc(diag_zero, 1)
            pool.wait_ge(diag_zero, 2)
            pool.affine_select(out=ident[:], in_=ident[:], compare_op=ALU.not_equal, fill=1.0, base=0,
                               pattern=[[-1, P]], channel_multiplier=1).then_inc(ident_ready, 1)

            def normalise(j, r):
                pool.wait_ge(inv_ready, j + 1)
                if past(j, 2):
                    pool.wait_ge(pt_ready, j - 1)
                for h in range(2):
                    rows = slice(h * M, (h + 1) * M)
                    pool.tensor_tensor(diag[rows, r % 2, :, h * M:(h + 1) * M], probs[rows, r % 2],
                                       row_inv[rows, r % 2].broadcast_to([M, T, M]), ALU.mult)\
                        .then_inc(diag_ready, 1)

            def step(i, k, r):
                if exists(i):
                    normalise(i, r)

            run(pool, step, 0, PAIRS)


_INS = ['r_x', 'L0_rec_Wq', 'L0_rec_Wk', 'L0_rec_Wv', 'L0_rec_Wr']


def kernel(**inputs):
    import numpy as _np
    import concourse.bacc as _bacc
    from concourse import mybir as _mybir
    from concourse.bass_utils import run_bass_kernel_spmd as _run

    nc = _bacc.Bacc("TRN2", target_bir_lowering=False, num_devices=1)
    arrays, args = {}, []
    for name in _INS:
        a = _np.ascontiguousarray(inputs[name])
        arrays[f"in_{name}_dram"] = a
        args.append(nc.dram_tensor(f"in_{name}_dram", a.shape, _mybir.dt.from_np(a.dtype), kind="ExternalInput").ap())
    x = arrays["in_r_x_dram"]
    args.append(nc.dram_tensor("out_0_dram", x.shape, _mybir.dt.from_np(x.dtype), kind="ExternalOutput").ap())
    recommender_self_attention(nc, *args)
    r = _run(nc, [arrays], core_ids=[0])
    return r.results[0]["out_0_dram"]
```

```python
from contextlib import ExitStack

import concourse.bass as bass
from concourse import mybir


def recommender_self_attention(
    nc: bass.Bass,
    x: bass.AP,
    Wq: bass.AP,
    Wk: bass.AP,
    Wv: bass.AP,
    Wr: bass.AP,
    out: bass.AP,
):
    fp32 = mybir.dt.float32
    fp32r = mybir.dt.float32r
    ALU = mybir.AluOpType
    ACT = mybir.ActivationFunctionType
    AX = mybir.AxisListType

    B, M, D = x.shape
    P = 128
    T = 2
    PAIRS = B * M // (P * T)
    C = 2
    SLOTS = 3
    U = C * SLOTS
    SC, RC, VC, PC = 0, P, 2 * P, 3 * P
    W3 = 3 * P
    ROUND_A = 2
    ROUND_Z = (PAIRS - 2) // U

    x_chunks = x.flatten_outer_dims().rearrange("(c t p) d -> c p t d", p=P, t=C * T)
    out_chunks = out.flatten_outer_dims().rearrange("(c t p) d -> c p t d", p=P, t=C * T)

    with ExitStack() as ctx:
        def sb(name, shape, dtype=fp32):
            return ctx.enter_context(nc.sbuf_tensor(name, shape, dtype))

        def sem(name):
            return ctx.enter_context(nc.semaphore(name))

        w_in = sb("w_in", [P, 4, D])
        w_t = sb("w_t", [P, 2, D])
        ident = sb("ident", [P, P])
        g_hi = sb("g_hi", [P, D], fp32r)
        g_lo = sb("g_lo", [P, D], fp32r)
        x_in = sb("x_in", [P, SLOTS, C * T, D])
        xt_hi = sb("xt_hi", [P, 3, T * P], fp32r)
        xt_lo = sb("xt_lo", [P, 3, T * P], fp32r)
        mv_hi = sb("mv_hi", [P, 2, T, W3], fp32r)
        mv_lo = sb("mv_lo", [P, 2, T, W3], fp32r)
        scores = sb("scores", [P, 2, T, M])
        shifted = sb("shifted", [P, 2, T, M])
        probs = sb("probs", [P, 2, T, M])
        row_max = sb("row_max", [P, 2, T, 1])
        row_sum = sb("row_sum", [P, 2, T, 1])
        row_inv = sb("row_inv", [P, 2, T, 1])
        p_norm = sb("p_norm", [P, 2, T, M])
        diag_t = sb("diag_t", [P, 2, T, P])
        v_sb = sb("v_sb", [P, 3, T, D])
        y_out = sb("y_out", [P, SLOTS, C * T, D])

        xt_ps = ctx.enter_context(nc.psum_tensor("xt_ps", [P, 512], fp32))
        t_ps = ctx.enter_context(nc.psum_tensor("t_ps", [P, 512], fp32))
        prod = ctx.enter_context(nc.psum_tensor("prod", [P, 3, T, 512], fp32))

        weights_loaded = sem("weights_loaded")
        ident_ready = sem("ident_ready")
        zeros_ready = sem("zeros_ready")
        w_t_ready = sem("w_t_ready")
        w_t_copied = sem("w_t_copied")
        g_ready = sem("g_ready")
        g_hi_ready = sem("g_hi_ready")
        w_hi_ready = sem("w_hi_ready")
        split_ready = sem("split_ready")
        x_loaded = [sem(f"x_loaded_{s}") for s in range(SLOTS)]
        y_stored = [sem(f"y_stored_{s}") for s in range(SLOTS)]
        xt_ready = sem("xt_ready")
        xt_hi_ready = sem("xt_hi_ready")
        xt_lo_ready = sem("xt_lo_ready")
        t_ready = sem("t_ready")
        t_hi_ready = sem("t_hi_ready")
        t_lo_ready = sem("t_lo_ready")
        prod_ready = sem("prod_ready")
        scores_copied = sem("scores_copied")
        v_copied = sem("v_copied")
        max_ready = sem("max_ready")
        shift_ready = sem("shift_ready")
        exp_ready = sem("exp_ready")
        sum_ready = sem("sum_ready")
        inv_ready = sem("inv_ready")
        p_ready = sem("p_ready")
        pt_ready = sem("pt_ready")
        pt0_copied = sem("pt0_copied")
        pt1_copied = sem("pt1_copied")
        y_ready = sem("y_ready")
        y0_copied = sem("y0_copied")
        y1_copied = sem("y1_copied")

        block = ctx.enter_context(nc.Block())

        def exists(j):
            return not isinstance(j, int) or 0 <= j < PAIRS

        def past(j, n):
            return not isinstance(j, int) or j >= n

        def run(engine, step, first, end):
            for i in range(first, ROUND_A * U):
                step(i, i // U, i % U)
            with engine.Fori(ROUND_A, ROUND_Z) as k:
                i = engine.snap(k * U)
                for r in range(U):
                    step(i + r, k, r)
            for i in range(ROUND_Z * U, end):
                step(i, i // U, i % U)

        @block.sync
        def _(sp):
            for n, w in enumerate((Wq, Wk, Wr, Wv)):
                sp.dma_start(w_in[:, n, :], w).then_inc(weights_loaded, 16)

            def load(c, s):
                sp.dma_start(x_in[:, s], x_chunks[c]).then_inc(x_loaded[s], 16)

            def store(c, s):
                sp.wait_ge(y0_copied, (c + 1) * C)
                sp.wait_ge(y1_copied, (c + 1) * C)
                sp.dma_start(out_chunks[c], y_out[:, s]).then_inc(y_stored[s], 16)

            def reload(c, s):
                sp.wait_ge(xt_ready, (c + 1 - SLOTS) * C)
                load(c, s)

            chunks = PAIRS // C
            for c in range(SLOTS):
                load(c, c)
            for c in range(SLOTS, 2 * SLOTS):
                reload(c, c - SLOTS)
            loop_end = chunks // SLOTS * SLOTS
            with sp.Fori(2, chunks // SLOTS) as k:
                for s in range(SLOTS):
                    store((k - 2) * SLOTS + s, s)
                    reload(k * SLOTS + s, s)
            for c in range(loop_end, chunks):
                reload(c, c % SLOTS)
            for c in range(loop_end - 2 * SLOTS, chunks):
                store(c, c % SLOTS)
            for s in range(SLOTS):
                sp.wait_ge(y_stored[s], 16 * len(range(s, chunks, SLOTS)))

        @block.tensor
        def _(pe):
            pe.wait_ge(weights_loaded, 64)
            pe.wait_ge(ident_ready, 1)
            for n in range(2):
                last = pe.transpose(xt_ps[:, n * P:(n + 1) * P], w_in[:, n, :], ident[:])
            last.then_inc(w_t_ready, 1)
            pe.wait_ge(w_t_copied, 1)
            pe.matmul(t_ps[:, 0:D], w_t[:, 1, :], w_t[:, 0, :], start=True, stop=True).then_inc(g_ready, 1)
            pe.wait_ge(split_ready, 2)

            def transpose_x(j, k, r):
                if r % C == 0:
                    pe.wait_ge(x_loaded[r // C], k * 16 + 16)
                if past(j, 1):
                    pe.wait_ge(xt_lo_ready, j)
                for t in range(T):
                    last = pe.transpose(xt_ps[:, t * P:(t + 1) * P], x_in[:, r // C, r % C * T + t, :], ident[:])
                last.then_inc(xt_ready, 1)

            def project_t(j, r):
                pe.wait_ge(xt_hi_ready, j + 1)
                pe.wait_ge(xt_lo_ready, j + 1)
                if past(j, 1):
                    pe.wait_ge(t_lo_ready, j)
                o = t_ps[:, 0:T * P]
                pe.matmul(o, g_hi[:], xt_hi[:, r % 3], start=True, stop=False)
                pe.matmul(o, g_lo[:], xt_hi[:, r % 3], start=False, stop=False)
                pe.matmul(o, g_hi[:], xt_lo[:, r % 3], start=False, stop=True).then_inc(t_ready, 1)

            def transpose_p(j, r):
                pe.wait_ge(p_ready, j + 1)
                pe.wait_ge(v_copied, j + 1)
                pe.matmul(prod[:, r % 3, 0, PC:PC + P], p_norm[:, r % 2].rearrange("p a b -> p (a b)"), ident[:],
                          is_transpose=True, start=False, stop=True, skip_group_check=True).then_inc(pt_ready, 1)

            def product(j, r):
                pe.wait_ge(t_hi_ready, j + 1)
                pe.wait_ge(t_lo_ready, j + 1)
                for t in range(T):
                    if past(j, 3):
                        pe.wait_ge((y0_copied, y1_copied)[t], j - 2)
                    o = prod[:, r % 3, t, 0:W3]
                    xh = xt_hi[:, r % 3, t * P:(t + 1) * P]
                    xl = xt_lo[:, r % 3, t * P:(t + 1) * P]
                    pe.matmul(o, xh, mv_hi[:, r % 2, t], start=True, stop=False, skip_group_check=True)
                    pe.matmul(o, xh, mv_lo[:, r % 2, t], start=False, stop=False, skip_group_check=True)
                    last = pe.matmul(o, xl, mv_hi[:, r % 2, t], start=False, stop=False, skip_group_check=True)
                    last.then_inc(prod_ready, 1)

            def attend(j, r):
                pe.wait_ge(pt0_copied, j + 1)
                pe.wait_ge(pt1_copied, j + 1)
                for t in range(T):
                    pe.matmul(prod[:, r % 3, t, RC:RC + D], diag_t[:, r % 2, t], v_sb[:, r % 3, t],
                              start=False, stop=True, skip_group_check=True).then_inc(y_ready, 1)

            def step(i, k, r):
                if exists(i + 2):
                    transpose_x(i + 2, k + (r + 2) // U, (r + 2) % U)
                if exists(i + 1):
                    project_t(i + 1, (r + 1) % U)
                if exists(i - 2):
                    transpose_p(i - 2, (r - 2) % U)
                if exists(i):
                    product(i, r)
                if exists(i - 2):
                    attend(i - 2, (r - 2) % U)

            run(pe, step, -2, PAIRS + 2)

        @block.scalar
        def _(act):
            act.wait_ge(zeros_ready, 2)
            act.wait_ge(weights_loaded, 64)
            for s in range(2):
                for t in range(T):
                    last = act.copy(mv_hi[:, s, t, RC:W3], w_in[:, 2:4, :].rearrange("p a b -> p (a b)"))
            last.then_inc(w_hi_ready, 1)
            act.wait_ge(w_t_ready, 1)
            act.copy(w_t[:].rearrange("p a b -> p (a b)"), xt_ps[:, 0:2 * P]).then_inc(w_t_copied, 1)
            act.wait_ge(g_ready, 1)
            act.copy(g_hi[:], t_ps[:, 0:D]).then_inc(g_hi_ready, 1)

            def copy_scores(j, r):
                if past(j, 2):
                    act.wait_ge(shift_ready, j - 1)
                for t in range(T):
                    act.wait_ge(prod_ready, j * T + t + 1)
                    for b in range(2):
                        rows = slice(b * M, (b + 1) * M)
                        act.copy(scores[t * M:(t + 1) * M, r % 2, b], prod[rows, r % 3, t, rows])\
                           .then_inc(scores_copied, 1)

            def copy_v(j, r):
                if past(j, 3):
                    act.wait_ge(y_ready, (j - 2) * T)
                act.copy(v_sb[:, r % 3], prod[:, r % 3, :, VC:VC + D]).then_inc(v_copied, 1)

            def round_xt(j, r):
                act.wait_ge(xt_ready, j + 1)
                if past(j, 3):
                    act.wait_ge(prod_ready, (j - 2) * T)
                act.copy(xt_hi[:, r % 3], xt_ps[:, 0:T * P]).then_inc(xt_hi_ready, 1)

            def round_t(j, r):
                act.wait_ge(t_ready, j + 1)
                if past(j, 2):
                    act.wait_ge(prod_ready, (j - 1) * T)
                act.copy(mv_hi[:, r % 2, :, SC:SC + P],
                         t_ps[:, 0:T * P].rearrange("p (t c) -> p t c", t=T)).then_inc(t_hi_ready, 1)

            def exponentials(j, r):
                act.wait_ge(shift_ready, j + 1)
                if past(j, 2):
                    act.wait_ge(p_ready, j - 1)
                act.activation(probs[:, r % 2], shifted[:, r % 2], ACT.Exp).then_inc(exp_ready, 1)

            def copy_pt(j, r):
                act.wait_ge(pt_ready, j + 1)
                if past(j, 2):
                    act.wait_ge(y_ready, (j - 1) * T)
                rows = slice(0, M)
                act.copy(diag_t[rows, r % 2, :, rows],
                         prod[rows, r % 3, 0, PC:PC + P].rearrange("p (t m) -> p t m", t=T)).then_inc(pt0_copied, 1)

            def finish(j, k, r):
                act.wait_ge(y_ready, j * T + 1)
                if r % C == 0 and past(j, U):
                    act.wait_ge(y_stored[r // C], k * 16)
                act.activation(y_out[:, r // C, r % C * T], prod[:, r % 3, 0, RC:RC + D],
                               ACT.Relu).then_inc(y0_copied, 1)

            def step(i, k, r):
                if exists(i - 1):
                    copy_scores(i - 1, (r - 1) % U)
                if exists(i - 3):
                    finish(i - 3, k + (r - 3) // U, (r - 3) % U)
                if exists(i + 2):
                    round_xt(i + 2, (r + 2) % U)
                if exists(i - 1):
                    exponentials(i - 1, (r - 1) % U)
                if exists(i + 1):
                    round_t(i + 1, (r + 1) % U)
                if exists(i - 2):
                    copy_pt(i - 2, (r - 2) % U)
                if exists(i - 1):
                    copy_v(i - 1, (r - 1) % U)

            run(act, step, -2, PAIRS + 3)

        @block.vector
        def _(dve):
            dve.wait_ge(zeros_ready, 2)
            dve.wait_ge(w_hi_ready, 1)
            for s in range(2):
                for t in range(T):
                    last = dve.tensor_tensor(mv_lo[:, s, t, RC:W3], w_in[:, 2:4, :].rearrange("p a b -> p (a b)"),
                                             mv_hi[:, s, t, RC:W3], ALU.subtract)
            last.then_inc(split_ready, 1)
            dve.wait_ge(g_hi_ready, 1)
            dve.tensor_tensor(g_lo[:], t_ps[:, 0:D], g_hi[:], ALU.subtract).then_inc(split_ready, 1)

            def maximum(j, r):
                dve.wait_ge(scores_copied, j * 4 + 4)
                dve.tensor_reduce(row_max[:, r % 2], scores[:, r % 2], AX.X, ALU.max).then_inc(max_ready, 1)

            def shift(j, r):
                dve.wait_ge(max_ready, j + 1)
                dve.tensor_tensor(shifted[:, r % 2], scores[:, r % 2],
                                  row_max[:, r % 2].broadcast_to([P, T, M]), ALU.subtract).then_inc(shift_ready, 1)

            def rest_of_xt(j, r):
                dve.wait_ge(xt_hi_ready, j + 1)
                dve.tensor_tensor(xt_lo[:, r % 3], xt_ps[:, 0:T * P], xt_hi[:, r % 3],
                                  ALU.subtract).then_inc(xt_lo_ready, 1)

            def rest_of_t(j, r):
                dve.wait_ge(t_hi_ready, j + 1)
                dve.tensor_tensor(mv_lo[:, r % 2, :, SC:SC + P], t_ps[:, 0:T * P].rearrange("p (t c) -> p t c", t=T),
                                  mv_hi[:, r % 2, :, SC:SC + P], ALU.subtract).then_inc(t_lo_ready, 1)

            def sums(j, r):
                dve.wait_ge(exp_ready, j + 1)
                dve.tensor_reduce(row_sum[:, r % 2], probs[:, r % 2], AX.X, ALU.add).then_inc(sum_ready, 1)

            def inverses(j, r):
                dve.wait_ge(sum_ready, j + 1)
                dve.reciprocal(row_inv[:, r % 2], row_sum[:, r % 2]).then_inc(inv_ready, 1)

            def finish(j, k, r):
                dve.wait_ge(y_ready, j * T + 2)
                if r % C == 0 and past(j, U):
                    dve.wait_ge(y_stored[r // C], k * 16)
                dve.tensor_scalar(y_out[:, r // C, r % C * T + 1], prod[:, r % 3, 1, RC:RC + D],
                                  0.0, None, ALU.max).then_inc(y1_copied, 1)

            def copy_pt(j, r):
                dve.wait_ge(pt_ready, j + 1)
                if past(j, 2):
                    dve.wait_ge(y_ready, (j - 1) * T)
                rows = slice(M, 2 * M)
                dve.tensor_copy(diag_t[rows, r % 2, :, rows],
                                prod[rows, r % 3, 0, PC:PC + P].rearrange("p (t m) -> p t m", t=T))\
                   .then_inc(pt1_copied, 1)

            def step(i, k, r):
                if exists(i - 1):
                    maximum(i - 1, (r - 1) % U)
                    shift(i - 1, (r - 1) % U)
                if exists(i - 3):
                    finish(i - 3, k + (r - 3) // U, (r - 3) % U)
                if exists(i - 2):
                    copy_pt(i - 2, (r - 2) % U)
                if exists(i - 1):
                    sums(i - 1, (r - 1) % U)
                if exists(i + 2):
                    rest_of_xt(i + 2, (r + 2) % U)
                if exists(i - 1):
                    inverses(i - 1, (r - 1) % U)
                if exists(i + 1):
                    rest_of_t(i + 1, (r + 1) % U)

            run(dve, step, -2, PAIRS + 3)

        @block.gpsimd
        def _(pool):
            pool.memset(ident[:], 0.0).then_inc(zeros_ready, 1)
            pool.memset(diag_t[:], 0.0).then_inc(zeros_ready, 1)
            pool.wait_ge(zeros_ready, 2)
            pool.affine_select(out=ident[:], in_=ident[:], compare_op=ALU.not_equal, fill=1.0, base=0,
                               pattern=[[-1, P]], channel_multiplier=1).then_inc(ident_ready, 1)

            def normalise(j, r):
                pool.wait_ge(inv_ready, j + 1)
                if past(j, 2):
                    pool.wait_ge(pt_ready, j - 1)
                pool.tensor_tensor(p_norm[:, r % 2], probs[:, r % 2],
                                   row_inv[:, r % 2].broadcast_to([P, T, M]), ALU.mult).then_inc(p_ready, 1)

            def step(i, k, r):
                if exists(i):
                    normalise(i, r)

            run(pool, step, 0, PAIRS)


_INS = ['r_x', 'L0_rec_Wq', 'L0_rec_Wk', 'L0_rec_Wv', 'L0_rec_Wr']


def kernel(**inputs):
    import numpy as _np
    import concourse.bacc as _bacc
    from concourse import mybir as _mybir
    from concourse.bass_utils import run_bass_kernel_spmd as _run

    nc = _bacc.Bacc("TRN2", target_bir_lowering=False, num_devices=1)
    arrays, args = {}, []
    for name in _INS:
        a = _np.ascontiguousarray(inputs[name])
        arrays[f"in_{name}_dram"] = a
        args.append(nc.dram_tensor(f"in_{name}_dram", a.shape, _mybir.dt.from_np(a.dtype), kind="ExternalInput").ap())
    x = arrays["in_r_x_dram"]
    args.append(nc.dram_tensor("out_0_dram", x.shape, _mybir.dt.from_np(x.dtype), kind="ExternalOutput").ap())
    recommender_self_attention(nc, *args)
    r = _run(nc, [arrays], core_ids=[0])
    return r.results[0]["out_0_dram"]
```
